# Optimizing a Trainium2 kernel written in Bass

```python
import numpy as np
import jax
import jax.numpy as jnp

def _softmax(x, axis=-1):
    return jax.nn.softmax(x, axis=axis)

def _gelu(x):
    return jax.nn.gelu(x, approximate=True)

def _silu(x):
    return jax.nn.silu(x)

def _sigmoid(x):
    return jax.nn.sigmoid(x)

def _layernorm(x, axis=-1, eps=1e-05):
    m = jnp.mean(x, axis=axis, keepdims=True)
    v = jnp.var(x, axis=axis, keepdims=True)
    return (x - m) / jnp.sqrt(v + eps)

def _scatter_add(tgt, idx, src, axis=0):
    return tgt.at[idx].add(src)

def _segment_sum(src, seg, n):
    return jax.ops.segment_sum(src, seg, n)
kernel_name = 'mk_cond_resid_d2_seqx_r4_ab3681'

def setup_inputs(seed: int=0):
    np.random.seed(seed)
    _w = jnp.asarray

    def _rec_inputs():
        import jax
        import jax.numpy as jnp
        _rk = jax.random.key(seed)
        x = -0.0003929 + 0.9999 * jax.random.normal(jax.random.fold_in(_rk, 1), (64, 64, 512), jnp.float32)
        _lenS = 64 - jax.random.randint(jax.random.fold_in(_rk, 7), (64,), 0, max(1, 64 // 4) + 1, jnp.int32)
        _lenS2 = 64 - jax.random.randint(jax.random.fold_in(_rk, 8), (64,), 0, max(1, 64 // 4) + 1, jnp.int32)
        itok_B_0_7 = jax.random.randint(jax.random.fold_in(_rk, 11), (64,), 0, 8, jnp.int32)
        return (x, itok_B_0_7)
    x, itok_B_0_7 = _rec_inputs()

    def _L0_cond_setup():
        import jax, jax.numpy as jnp
        import numpy as np

        def _lora_linear(x, W, A, B, adapter_indices):
            base = jnp.einsum('bsd,df->bsf', x, W)
            Ai = A[adapter_indices]
            Bi = B[adapter_indices]
            lora = jnp.einsum('bsr,brf->bsf', jnp.einsum('bsd,bdr->bsr', x, Ai), Bi)
            return base + lora
        key = jax.random.key(seed)
        ks = jax.random.split(key, 10)
        H, I, N, R = (512, 2048, 8, 16)
        B, S = (4, 512)
        std_h = 1.0 / np.sqrt(H)
        std_i = 1.0 / np.sqrt(I)
        x = jax.random.normal(ks[0], (B, S, H), dtype=jnp.float32)
        adapter_indices = jax.random.randint(ks[1], (B,), 0, N, dtype=jnp.int32)
        Wg = jax.random.normal(ks[2], (H, I), dtype=jnp.float32) * std_h
        Wu = jax.random.normal(ks[3], (H, I), dtype=jnp.float32) * std_h
        Wd = jax.random.normal(ks[4], (I, H), dtype=jnp.float32) * std_i
        Ag = jax.random.normal(ks[5], (N, H, R), dtype=jnp.float32) * std_h
        Bg = jnp.zeros((N, R, I), dtype=jnp.float32) + 0.01
        Au = jax.random.normal(ks[6], (N, H, R), dtype=jnp.float32) * std_h
        Bu = jnp.zeros((N, R, I), dtype=jnp.float32) + 0.01
        Ad = jax.random.normal(ks[7], (N, I, R), dtype=jnp.float32) * std_i
        Bd = jnp.zeros((N, R, H), dtype=jnp.float32) + 0.01
        return {'x': x, 'Wg': Wg, 'Wu': Wu, 'Wd': Wd, 'Ag': Ag, 'Bg': Bg, 'Au': Au, 'Bu': Bu, 'Ad': Ad, 'Bd': Bd, 'adapter_indices': adapter_indices}
    _L0_cond_all = _L0_cond_setup()
    _L0_cond_in = {k: v for k, v in _L0_cond_all.items() if k in ('Wg', 'Wu', 'Wd', 'Ag', 'Bg', 'Au', 'Bu', 'Ad', 'Bd')}
    del _L0_cond_all

    def _L1_cond_setup():
        import jax, jax.numpy as jnp
        import numpy as np
        B, C, D, T, N_SUBJECTS = (128, 64, 64, 512, 8)
        key = jax.random.key(seed)
        kx, ks, kw = jax.random.split(key, 3)
        x = jax.random.normal(kx, (B, C, T), dtype=jnp.float32)
        subjects = jax.random.randint(ks, (B,), 0, N_SUBJECTS, dtype=jnp.int64)
        weights = jax.random.normal(kw, (N_SUBJECTS, C, D), dtype=jnp.float32) * (1.0 / C ** 0.5)
        return {'x': x, 'subjects': subjects, 'weights': weights}
    _L1_cond_all = _L1_cond_setup()
    _L1_cond_in = {k: v for k, v in _L1_cond_all.items() if k in ('weights',)}
    del _L1_cond_all
    return {'x': x, 'itok_B_0_7': itok_B_0_7, 'L0_cond_Wg': _L0_cond_in['Wg'], 'L0_cond_Wu': _L0_cond_in['Wu'], 'L0_cond_Wd': _L0_cond_in['Wd'], 'L0_cond_Ag': _L0_cond_in['Ag'], 'L0_cond_Bg': _L0_cond_in['Bg'], 'L0_cond_Au': _L0_cond_in['Au'], 'L0_cond_Bu': _L0_cond_in['Bu'], 'L0_cond_Ad': _L0_cond_in['Ad'], 'L0_cond_Bd': _L0_cond_in['Bd'], 'L1_cond_weights': _L1_cond_in['weights']}

def reference(x, itok_B_0_7, L0_cond_Wg, L0_cond_Wu, L0_cond_Wd, L0_cond_Ag, L0_cond_Bg, L0_cond_Au, L0_cond_Bu, L0_cond_Ad, L0_cond_Bd, L1_cond_weights):
    import jax
    import jax.numpy as jnp

    def _L0_cond_ref(x, Wg, Wu, Wd, Ag, Bg, Au, Bu, Ad, Bd, adapter_indices):
        import jax, jax.numpy as jnp
        import numpy as np

        def _lora_linear(x, W, A, B, adapter_indices):
            base = jnp.einsum('bsd,df->bsf', x, W)
            Ai = A[adapter_indices]
            Bi = B[adapter_indices]
            lora = jnp.einsum('bsr,brf->bsf', jnp.einsum('bsd,bdr->bsr', x, Ai), Bi)
            return base + lora
        gate = _lora_linear(x, Wg, Ag, Bg, adapter_indices)
        up = _lora_linear(x, Wu, Au, Bu, adapter_indices)
        h = jax.nn.silu(gate) * up
        return _lora_linear(h, Wd, Ad, Bd, adapter_indices)

    def _L1_cond_ref(x, subjects, weights):
        import jax, jax.numpy as jnp
        import numpy as np
        B, C, D, T, N_SUBJECTS = (128, 64, 64, 512, 8)
        w = weights[subjects]
        out = jnp.einsum('bct,bcd->bdt', x, w)
        return out
    x = x + _L0_cond_ref(x, L0_cond_Wg, L0_cond_Wu, L0_cond_Wd, L0_cond_Ag, L0_cond_Bg, L0_cond_Au, L0_cond_Bu, L0_cond_Ad, L0_cond_Bd, itok_B_0_7)
    x = x + _L1_cond_ref(x, itok_B_0_7, L1_cond_weights)
    return x

_drawn_inputs = setup_inputs


def setup_inputs(seed=0):
    import zlib

    import numpy as np

    out = dict(_drawn_inputs(seed))
    spreads = {'L0_cond_Bg': (0.009999999776482582, 0.2),
     'L0_cond_Bu': (0.009999999776482582, 0.2),
     'L0_cond_Bd': (0.009999999776482582, 0.2)}
    factors = {}
    for name, (base, spread) in spreads.items():
        noise = np.random.default_rng([zlib.crc32(name.encode()), seed]).standard_normal(out[name].shape)
        drawn = base * np.exp(spread * noise) if base else spread * noise
        out[name] = jnp.asarray(drawn.astype(out[name].dtype))
    for name, factor in factors.items():
        out[name] = (out[name] * factor).astype(out[name].dtype)
    return out
```

```python
from contextlib import ExitStack

import concourse.bass as bass
from concourse import mybir

F32 = mybir.dt.float32
F32R = mybir.dt.float32r
I32 = mybir.dt.int32
ALU = mybir.AluOpType
ACT = mybir.ActivationFunctionType

P = 128
BATCH, SEQ, D, I = 64, 64, 512, 2048
ADAPTERS, RANK = 8, 16
TOK = 512
GROUPS = BATCH * SEQ // TOK
TILES = TOK // P
PER = TOK // SEQ
KT = D // P
CHUNKS = I // P
STEPS = GROUPS * CHUNKS
HEAD = 4
GW = KT * P
PACK = 2 * GW + D
QS = 4
QUADS = PER // QS
QT = QS * SEQ
QR = QS * RANK
HALF = CHUNKS // 2
BW = 2 * P
B_DMAS = 16 * PER * 2


def cond_resid_kernel(nc, x, xt, idx, packed, a_gu, a_d, b_gu, b_d, w1, slot_mask, out):
    ctx = ExitStack()
    with ctx:
        def sb(name, shape, dt=F32):
            return ctx.enter_context(nc.sbuf_tensor(name, shape, dt))

        def sem(name):
            return ctx.enter_context(nc.semaphore(name))

        raw = [sb(f"raw{i}", [P, PACK]) for i in range(2)]
        w_hi = [sb(f"w_hi{i}", [P, PACK], F32R) for i in range(2)]
        w_lo = [sb(f"w_lo{i}", [P, PACK], F32R) for i in range(2)]
        xt_raw = sb("xt_raw", [P, KT * TOK])
        xt_hi = [sb(f"xt_hi{i}", [P, KT * TOK], F32R) for i in range(2)]
        xt_lo = [sb(f"xt_lo{i}", [P, KT * TOK], F32R) for i in range(2)]
        a_all = sb("a_all", [P, ADAPTERS, KT * 2, RANK])
        aq_raw = sb("aq_raw", [P, QUADS, KT * 2, QS, RANK])
        aq_hi = sb("aq_hi", [P, QUADS * KT * P], F32R)
        aq_lo = sb("aq_lo", [P, QUADS * KT * P], F32R)
        ad_all = sb("ad_all", [P, ADAPTERS, CHUNKS, RANK])
        adq_raw = sb("adq_raw", [P, CHUNKS, QUADS, QS, RANK])
        ad_hl = [sb(f"ad_hl{i}", [P, QUADS, 2, QR], F32R) for i in range(2)]
        bq_raw = sb("bq_raw", [P, QUADS, CHUNKS * BW])
        bq_hi = [sb(f"bq_hi{i}", [P, QUADS, BW], F32R) for i in range(2)]
        bq_lo = [sb(f"bq_lo{i}", [P, QUADS, BW], F32R) for i in range(2)]
        bd_raw = sb("bd_raw", [P, QUADS, D])
        bd_hi = sb("bd_hi", [P, QUADS, D], F32R)
        bd_lo = sb("bd_lo", [P, QUADS, D], F32R)
        t_f = sb("t_f", [P, TOK])
        t_st = [[sb(f"t_st{u}{i}", [P, TOK], F32R) for i in range(2)] for u in range(2)]
        td_b = t_f[0:QR, :]
        td_f = sb("td_f", [QR, TOK])
        td_st = sb("td_st", [P, TOK], F32R)
        act_g = sb("act_g", [P, TOK])
        h_f = sb("h_f", [P, TOK])
        h_hi = [sb(f"h_hi{i}", [P, TOK], F32R) for i in range(2)]
        h_lo = [sb(f"h_lo{i}", [P, TOK], F32R) for i in range(2)]
        x1 = sb("x1", [P, TILES, D])
        y = sb("y", [P, TILES, D])
        mix = sb("mix", [P, TILES, P])
        idx_i = sb("idx_i", [1, BATCH], I32)
        mask = sb("mask", [P, PER])

        gate_ps = ctx.enter_context(nc.psum_tensor("gate_ps", [P, TOK], F32))
        up_ps = ctx.enter_context(nc.psum_tensor("up_ps", [P, TOK], F32))
        td_ps = ctx.enter_context(nc.psum_tensor("td_ps", [P, TOK], F32))
        misc_ps = ctx.enter_context(nc.psum_tensor("misc_ps", [P, TOK], F32))
        out_ps = [ctx.enter_context(nc.psum_tensor(f"out_ps{j}", [P, D], F32)) for j in range(TILES)]

        LAST_BANKS = [misc_ps, gate_ps, up_ps, td_ps]

        idx_in = sem("idx_in")
        a_in = sem("a_in")
        ad_in = sem("ad_in")
        mask_in = sem("mask_in")
        raw_in = [sem(f"raw_in{i}") for i in range(2)]
        xt_in = sem("xt_in")
        x_in = sem("x_in")
        mix_in = sem("mix_in")
        y_out = [sem(f"y_out{j}") for j in range(TILES)]
        hi_done = {n: sem(f"hi_{n}") for n in "gud"}
        lo_done = {n: sem(f"lo_{n}") for n in "gud"}
        a_gathered = sem("a_gathered")
        ad_gathered = sem("ad_gathered")
        bq_in = sem("bq_in")
        bd_in = sem("bd_in")
        aq_hi_done = sem("aq_hi_done")
        aq_lo_done = sem("aq_lo_done")
        bd_hi_done = sem("bd_hi_done")
        bd_lo_done = sem("bd_lo_done")
        mix_zero = sem("mix_zero")
        wg_hi_done = sem("wg_hi_done")
        wg_lo_done = sem("wg_lo_done")
        xt_hi_done = sem("xt_hi_done")
        xt_lo_done = sem("xt_lo_done")
        gate_done = sem("gate_done")
        up_done = sem("up_done")
        down_done = sem("down_done")
        silu_done = sem("silu_done")
        h_done = sem("h_done")
        h_hi_done = sem("h_hi_done")
        h_lo_done = sem("h_lo_done")
        t_done = sem("t_done")
        t_masked = sem("t_masked")
        t_hi_done = sem("t_hi_done")
        t_lo_done = sem("t_lo_done")
        td_done = sem("td_done")
        td_b_done = sem("td_b_done")
        td_sum = sem("td_sum")
        td_masked = sem("td_masked")
        td_hi_done = sem("td_hi_done")
        td_free = sem("td_free")
        out_done = sem("out_done")
        x1_done = sem("x1_done")
        mixed = sem("mixed")
        y_done = sem("y_done")

        COLS = {"g": (0, GW), "u": (GW, 2 * GW), "d": (2 * GW, PACK)}

        def run_groups(eng, chunk, first, last):
            def head(g, par, fin, prep):
                for c in range(HEAD):
                    chunk(g, par, c, c % 2, fin, prep)

            def rest(g, par, end=0):
                with eng.Fori(0, (CHUNKS - HEAD) // 2 - end) as p:
                    for k in range(2):
                        chunk(g, par, p * 2 + (HEAD + k), k, False, False)
                for c in range(CHUNKS - 2 * end, CHUNKS):
                    chunk(g, par, c, c % 2, False, False)

            first()
            head(0, 0, False, True)
            with eng.Fori(0, GROUPS // 2 - 1) as it:
                rest(it * 2, 0)
                head(it * 2 + 1, 1, True, True)
                rest(it * 2 + 1, 1)
                head(it * 2 + 2, 0, True, True)
            rest(GROUPS - 2, 0)
            head(GROUPS - 1, 1, True, False)
            rest(GROUPS - 1, 1, end=1)
            last()

        def chunk_of(eng, s):
            return s % CHUNKS if isinstance(s, int) else eng.snap(s % CHUNKS)

        def adq_of(eng, s):
            return adq_raw[:, bass.ds(chunk_of(eng, s), 1), :, :, :].rearrange("p a q s r -> p (a q) (s r)")

        def number(eng, g, b):
            at = idx_i[0:1, b:b + 1] if isinstance(g, int) and g == 0 else idx_i[0:1, bass.ds(g * PER + b, 1)]
            return eng.value_load(at, min_val=0, max_val=ADAPTERS - 1)

        def gather_b(eng, n, b, c0, c1):
            for h in range(2):
                r = h * QR + (b % QS) * RANK
                eng.dma_start(bq_raw[r:r + RANK, b // QS, c0 * BW:c1 * BW],
                              b_gu[bass.ds(n, 1), :, c0 * BW:c1 * BW].rearrange("a r c -> (a r) c"))\
                   .then_inc(bq_in, 16)

        block = ctx.enter_context(nc.Block())

        @block.sync
        def _(sp):
            def load_weights(s):
                for k in range(2):
                    sp.wait_ge(lo_done["d"], s + (k - 1))
                    src = packed[s + k] if isinstance(s, int) else \
                        packed[bass.ds(chunk_of(sp, s + k), 1)].rearrange("a p n -> (a p) n")
                    sp.dma_start(raw[k][:, :], src).then_inc(raw_in[k], 16)

            def gather_half(g, half):
                n = number(sp, g, 0)
                sp.wait_ge(bq_in, g * (2 * B_DMAS) + (half + 1) * B_DMAS)
                for b in range(PER):
                    n = n if b == 0 else number(sp, g, b)
                    gather_b(sp, n, b, half * HALF, (half + 1) * HALF)

            sp.dma_start(raw[0][:, :], packed[0]).then_inc(raw_in[0], 16)
            sp.wait_ge(idx_in, 16)
            for b in range(PER):
                gather_b(sp, number(sp, 0, b), b, 0, 2)
            sp.dma_start(raw[1][:, :], packed[1]).then_inc(raw_in[1], 16)
            sp.wait_ge(bq_in, B_DMAS)
            for b in range(PER):
                gather_b(sp, number(sp, 0, b), b, 2, HALF)
            load_weights(2)
            gather_half(0, 1)
            with sp.Fori(2, HALF // 2 + 1) as p:
                load_weights(p * 2)
            gather_half(1, 0)
            with sp.Fori(0, GROUPS - 2) as g:
                with sp.Fori(HALF // 2 + 1, CHUNKS // 2 + 1) as p:
                    load_weights(g * CHUNKS + p * 2)
                gather_half(g + 1, 1)
                with sp.Fori(1, HALF // 2 + 1) as p:
                    load_weights((g + 1) * CHUNKS + p * 2)
                gather_half(g + 2, 0)
            last = (GROUPS - 2) * CHUNKS // 2
            with sp.Fori(last + HALF // 2 + 1, last + CHUNKS // 2 + 1) as p:
                load_weights(p * 2)
            gather_half(GROUPS - 1, 1)
            with sp.Fori(last + CHUNKS // 2 + 1, STEPS // 2) as p:
                load_weights(p * 2)

        @block.gpsimd
        def _(pool):
            def one(t, g, dims="p n"):
                return t[g] if isinstance(g, int) else t[bass.ds(g, 1)].rearrange(f"a {dims} -> (a {dims[0]}) {dims[2:]}")

            def load_xt(g):
                if not (isinstance(g, int) and g == 0):
                    pool.wait_ge(xt_lo_done, g)
                pool.dma_start(xt_raw[:, :], one(xt, g)).then_inc(xt_in, 16)

            def gather_a(g):
                n = number(pool, g, 0)
                if not (isinstance(g, int) and g == 0):
                    pool.wait_ge(aq_lo_done, g)
                for b in range(PER):
                    n = n if b == 0 else number(pool, g, b)
                    pool.tensor_copy(aq_raw[:, b // QS, :, b % QS, :],
                                     a_all[:, bass.ds(n, 1), :, :].rearrange("p a k r -> p (a k) r"))\
                        .then_inc(a_gathered, 1)

            def gather_bd(g):
                n = number(pool, g, 0)
                if not (isinstance(g, int) and g == 0):
                    pool.wait_ge(bd_lo_done, g)
                for b in range(PER):
                    n = n if b == 0 else number(pool, g, b)
                    for h in range(2):
                        r = h * QR + (b % QS) * RANK
                        pool.dma_start(bd_raw[r:r + RANK, b // QS, :],
                                       b_d[bass.ds(n, 1)].rearrange("a r d -> (a r) d")).then_inc(bd_in, 16)

            def gather_ad(g, half):
                n = number(pool, g, 0)
                if not (isinstance(g, int) and g == 0):
                    pool.wait_ge(lo_done["d"], g * CHUNKS + (half - 1) * HALF)
                for b in range(PER):
                    n = n if b == 0 else number(pool, g, b)
                    pool.tensor_copy(adq_raw[:, half * HALF:(half + 1) * HALF, b // QS, b % QS, :],
                                     ad_all[:, bass.ds(n, 1), half * HALF:(half + 1) * HALF, :]
                                     .rearrange("p a k r -> p (a k) r")).then_inc(ad_gathered, 1)

            def load(g):
                if not (isinstance(g, int) and g == 0):
                    pool.wait_ge(y_done, g * TILES)
                    for j in range(TILES):
                        pool.wait_ge(y_out[j], g * 16)
                pool.dma_start(x1[:, :, :], one(x, g, "p j d")).then_inc(x_in, 16)
                for b in range(PER):
                    q = SEQ * (b % 2)
                    n = number(pool, g, b)
                    pool.dma_start(mix[q:q + SEQ, b // 2, q:q + SEQ],
                                   w1[bass.ds(n, 1)].rearrange("a c d -> (a c) d")).then_inc(mix_in, 16)

            def store(g):
                for j in range(TILES):
                    pool.wait_ge(y_done, g * TILES + (j + 1))
                    pool.dma_start(one(out, g, "p j d")[:, j, :], y[:, j, :]).then_inc(y_out[j], 16)

            def early(g):
                load_xt(g + 1)
                gather_a(g + 1)
                gather_ad(g, 1)
                gather_bd(g)

            load_xt(0)
            pool.memset(mix[:, :, :], 0.0).then_inc(mix_zero, 1)
            pool.wait_ge(idx_in, 16)
            pool.wait_ge(a_in, 16)
            gather_a(0)
            pool.wait_ge(ad_in, 16)
            gather_ad(0, 0)
            pool.wait_ge(mix_zero, 1)
            early(0)
            load(0)
            gather_ad(1, 0)
            with pool.Fori(1, GROUPS - 1) as g:
                early(g)
                store(g - 1)
                load(g)
                gather_ad(g + 1, 0)
            g = GROUPS - 1
            gather_ad(g, 1)
            gather_bd(g)
            store(g - 1)
            load(g)
            store(g)
            for j in range(TILES):
                pool.wait_ge(y_out[j], 16 * GROUPS)

        @block.scalar
        def _(act):
            act.dma_start(idx_i[0:1, :], idx).then_inc(idx_in, 16)
            act.dma_start(a_all[:, :, :, :], a_gu).then_inc(a_in, 16)
            act.dma_start(mask[:, :], slot_mask).then_inc(mask_in, 16)
            act.dma_start(ad_all[:, :, :, :], a_d).then_inc(ad_in, 16)

            def hi(dst, src):
                return act.activation(dst, src, ACT.Copy)

            def weights_hi(n, s, slot):
                a, b = COLS[n]
                early = isinstance(s, int) and s < 2
                if n == "g":
                    act.wait_ge(raw_in[slot], (s + 2 - slot) * 8)
                    act.wait_ge(bq_in, B_DMAS if isinstance(s, int) and s < 2 else (s // HALF + 2) * B_DMAS)
                if n == "d":
                    act.wait_ge(ad_gathered, (s // HALF + 1) * PER)
                if not early:
                    act.wait_ge({"g": gate_done, "u": up_done, "d": down_done}[n], s - 1)
                    if n == "g":
                        act.wait_ge(up_done, s - 1)
                m = hi(w_hi[slot][:, a:b], raw[slot][:, a:b])
                if n == "g":
                    m = hi(bq_hi[slot][:, :, :], bq_raw[:, :, bass.ds(chunk_of(act, s) * BW, BW)])
                if n == "d":
                    m = hi(ad_hl[slot][:, :, 0, :], adq_of(act, s))
                m.then_inc(hi_done[n], 1)

            def split_xt(g, par):
                act.wait_ge(xt_in, g * 16 + 16)
                hi(xt_hi[par][:, :], xt_raw[:, :]).then_inc(xt_hi_done, 1)

            def split_aq(g):
                act.wait_ge(a_gathered, g * PER + PER)
                if not (isinstance(g, int) and g == 0):
                    act.wait_ge(t_done, g)
                hi(aq_hi[:, :], aq_raw[:, :, :, :, :].rearrange("p q k s r -> p (q k s r)"))\
                    .then_inc(aq_hi_done, 1)

            def split_bd(g):
                act.wait_ge(bd_in, (g + 1) * B_DMAS)
                if not (isinstance(g, int) and g == 0):
                    act.wait_ge(out_done, g * TILES)
                hi(bd_hi[:, :, :], bd_raw[:, :, :]).then_inc(bd_hi_done, 1)

            def t_part(g, par):
                act.wait_ge(t_masked, g + 1)
                hi(t_st[0][par][0:QR, :], t_f[0:QR, :]).then_inc(t_hi_done, 1)
                hi(t_st[1][par][QR:P, :], t_f[QR:P, :]).then_inc(t_hi_done, 1)

            def td_copy(g):
                act.wait_ge(td_done, g + 1)
                act.activation(td_b, td_ps[QR:P, :], ACT.Copy).then_inc(td_b_done, 1)

            def td_part(g):
                act.wait_ge(td_masked, g + 1)
                hi(td_st[0:QR, :], td_f[:, :]).then_inc(td_hi_done, 1)

            def chunk(g, par, c, cpar, fin, prep):
                s = g * CHUNKS + c
                nxt = (cpar + 1) % 2
                at = c if isinstance(c, int) else -1
                more = not (isinstance(s, int) and s == STEPS - 1)
                if more:
                    weights_hi("g", s + 1, nxt)
                act.wait_ge(gate_done, s + 1)
                if not (isinstance(s, int) and s == 0):
                    act.wait_ge(h_done, s)
                act.activation(act_g[:, :], gate_ps[:, :], ACT.Silu).then_inc(silu_done, 1)
                if fin and at == 0:
                    td_copy(g - 1)
                if prep and at == 3:
                    t_part(g + 1, 1 - par)
                if more:
                    weights_hi("u", s + 1, nxt)
                if fin and at == 0:
                    td_part(g - 1)
                if more:
                    weights_hi("d", s + 1, nxt)
                if prep and at == 1:
                    split_aq(g + 1)
                    split_xt(g + 1, 1 - par)
                if at == 3:
                    split_bd(g)
                act.wait_ge(h_done, s + 1)
                hi(h_hi[cpar][:, :], h_f[:, :]).then_inc(h_hi_done, 1)

            def first():
                split_xt(0, 0)
                act.wait_ge(raw_in[0], 16)
                hi(w_hi[0][:, 0:GW], raw[0][:, 0:GW]).then_inc(wg_hi_done, 1)
                weights_hi("u", 0, 0)
                split_aq(0)
                t_part(0, 0)
                act.wait_ge(bq_in, B_DMAS)
                hi(bq_hi[0][:, :, :], bq_raw[:, :, 0:BW]).then_inc(hi_done["g"], 1)
                weights_hi("d", 0, 0)

            def last():
                td_copy(GROUPS - 1)
                td_part(GROUPS - 1)

            run_groups(act, chunk, first, last)

        @block.vector
        def _(dve):
            def lo(dst, src, hi):
                return dve.tensor_tensor(dst, src, hi.bitcast(F32), ALU.subtract)

            def weights_lo(n, s, slot):
                a, b = COLS[n]
                dve.wait_ge(hi_done[n], s + 1)
                m = lo(w_lo[slot][:, a:b], raw[slot][:, a:b], w_hi[slot][:, a:b])
                if n == "g":
                    m = lo(bq_lo[slot][:, :, :], bq_raw[:, :, bass.ds(chunk_of(dve, s) * BW, BW)],
                           bq_hi[slot][:, :, :])
                if n == "d":
                    m = lo(ad_hl[slot][:, :, 1, :], adq_of(dve, s), ad_hl[slot][:, :, 0, :])
                m.then_inc(lo_done[n], 1)

            def split_xt(g, par):
                dve.wait_ge(xt_hi_done, g + 1)
                lo(xt_lo[par][:, :], xt_raw[:, :], xt_hi[par][:, :]).then_inc(xt_lo_done, 1)

            def split_aq(g):
                dve.wait_ge(aq_hi_done, g + 1)
                lo(aq_lo[:, :], aq_raw[:, :, :, :, :].rearrange("p q k s r -> p (q k s r)"), aq_hi[:, :])\
                    .then_inc(aq_lo_done, 1)

            def split_bd(g):
                dve.wait_ge(bd_hi_done, g + 1)
                lo(bd_lo[:, :, :], bd_raw[:, :, :], bd_hi[:, :, :]).then_inc(bd_lo_done, 1)

            def masked(dst, src, rows):
                return dve.tensor_tensor(dst.rearrange("p (b t) -> p b t", t=SEQ),
                                         src.rearrange("p (b t) -> p b t", t=SEQ),
                                         mask[0:rows, :].unsqueeze(2).to_broadcast([rows, PER, SEQ]), ALU.mult)

            def t_mask(g):
                dve.wait_ge(t_done, g + 1)
                if not (isinstance(g, int) and g == 0):
                    dve.wait_ge(t_lo_done, g * 2)
                masked(t_f[:, :], misc_ps[:, :], P).then_inc(t_masked, 1)

            def t_part(g, par):
                dve.wait_ge(t_hi_done, g * 2 + 1)
                lo(t_st[0][par][QR:P, :], t_f[0:QR, :], t_st[0][par][0:QR, :]).then_inc(t_lo_done, 1)
                dve.wait_ge(t_hi_done, g * 2 + 2)
                lo(t_st[1][par][0:QR, :], t_f[QR:P, :], t_st[1][par][QR:P, :]).then_inc(t_lo_done, 1)

            def td_mask(g):
                dve.wait_ge(td_b_done, g + 1)
                dve.wait_ge(td_free, g + 1)
                dve.tensor_tensor(td_f[:, :], td_ps[0:QR, :], td_b, ALU.add).then_inc(td_sum, 1)
                dve.wait_ge(td_sum, g + 1)
                masked(td_f[:, :], td_f[:, :], QR).then_inc(td_masked, 1)

            def td_part(g):
                dve.wait_ge(td_hi_done, g + 1)
                lo(td_st[QR:P, :], td_f[:, :], td_st[0:QR, :]).then_inc(td_free, 1)

            def make_x1(g, j):
                if j == 0:
                    dve.wait_ge(x_in, g * 16 + 16)
                dve.wait_ge(out_done, g * TILES + (j + 1))
                dve.tensor_tensor(x1[:, j, :], out_ps[j][:, :], x1[:, j, :], ALU.add).then_inc(x1_done, 1)

            def make_y(g, j, bank=misc_ps):
                dve.wait_ge(mixed, g * TILES + (j + 1))
                dve.tensor_tensor(y[:, j, :], bank[:, :], x1[:, j, :], ALU.add).then_inc(y_done, 1)

            def first():
                dve.sem_inc(td_free, 1)
                split_xt(0, 0)
                dve.wait_ge(wg_hi_done, 1)
                lo(w_lo[0][:, 0:GW], raw[0][:, 0:GW], w_hi[0][:, 0:GW]).then_inc(wg_lo_done, 1)
                weights_lo("u", 0, 0)
                split_aq(0)
                dve.wait_ge(mask_in, 16)
                t_mask(0)
                t_part(0, 0)
                dve.wait_ge(hi_done["g"], 1)
                lo(bq_lo[0][:, :, :], bq_raw[:, :, 0:BW], bq_hi[0][:, :, :]).then_inc(lo_done["g"], 1)
                weights_lo("d", 0, 0)

            def chunk(g, par, c, cpar, fin, prep):
                s = g * CHUNKS + c
                nxt = (cpar + 1) % 2
                at = c if isinstance(c, int) else -1
                more = not (isinstance(s, int) and s == STEPS - 1)
                if prep and at == 2:
                    split_xt(g + 1, 1 - par)
                if more:
                    weights_lo("g", s + 1, nxt)
                if fin and at == 0:
                    td_mask(g - 1)
                if fin and at == 1:
                    make_y(g - 1, 0)
                if fin and at == 2:
                    make_y(g - 1, 3)
                if prep and at == 3:
                    t_mask(g + 1)
                    t_part(g + 1, 1 - par)
                if more:
                    weights_lo("u", s + 1, nxt)
                if fin and at == 0:
                    td_part(g - 1)
                if fin and at == 1:
                    make_y(g - 1, 1)
                if more:
                    weights_lo("d", s + 1, nxt)
                if prep and at == 1:
                    split_aq(g + 1)
                if at == 3:
                    split_bd(g)
                dve.wait_ge(silu_done, s + 1)
                dve.wait_ge(up_done, s + 1)
                if not (isinstance(g, int) and g == 0 and at == 0):
                    dve.wait_ge(h_lo_done, s)
                dve.tensor_tensor(h_f[:, :], up_ps[:, :], act_g[:, :], ALU.mult).then_inc(h_done, 1)
                dve.wait_ge(h_hi_done, s + 1)
                lo(h_lo[cpar][:, :], h_f[:, :], h_hi[cpar][:, :]).then_inc(h_lo_done, 1)
                if fin and at == 0:
                    for j in range(TILES):
                        make_x1(g - 1, j)
                if fin and at == 1:
                    make_y(g - 1, 2)

            def last():
                td_mask(GROUPS - 1)
                td_part(GROUPS - 1)
                for j in range(TILES):
                    make_x1(GROUPS - 1, j)
                for j in range(TILES):
                    make_y(GROUPS - 1, j, LAST_BANKS[j])

            run_groups(dve, chunk, first, last)

        @block.tensor
        def _(pe):
            def three(ps, st, mv, start, stop):
                pe.matmul(ps, st[0], mv[0], start=start, stop=False)
                pe.matmul(ps, st[0], mv[1], start=False, stop=False)
                return pe.matmul(ps, st[1], mv[0], start=False, stop=stop)

            def cols(pair, a, b):
                return pair[0][:, a:b], pair[1][:, a:b]

            def dense(ps, n, slot, par):
                w, xp = (w_hi[slot], w_lo[slot]), (xt_hi[par], xt_lo[par])
                a = COLS[n][0]
                for k in range(KT):
                    three(ps[:, :], cols(w, a + k * P, a + k * P + P), cols(xp, k * TOK, k * TOK + TOK),
                          k == 0, False)

            def lora(ps, u, slot, par):
                for part in (bq_hi, bq_lo):
                    for q in range(QUADS):
                        m = pe.matmul(ps[:, q * QT:(q + 1) * QT], part[slot][:, q, u * P:(u + 1) * P],
                                      t_st[u][par][:, q * QT:(q + 1) * QT], start=False,
                                      stop=part is bq_lo and q == QUADS - 1)
                return m

            def gate(s, slot, g, par, at):
                pe.wait_ge(lo_done["g"], s + 1)
                if at == 0:
                    pe.wait_ge(t_lo_done, g * 2 + 2)
                pe.wait_ge(silu_done, s)
                dense(gate_ps, "g", slot, par)
                lora(gate_ps, 0, slot, par).then_inc(gate_done, 1)

            def up(s, slot, par):
                pe.wait_ge(lo_done["u"], s + 1)
                pe.wait_ge(h_done, s)
                dense(up_ps, "u", slot, par)
                lora(up_ps, 1, slot, par).then_inc(up_done, 1)

            def step_0():
                pe.wait_ge(xt_lo_done, 1)
                pe.wait_ge(wg_lo_done, 1)
                dense(gate_ps, "g", 0, 0)
                lora_a(0, 0)
                pe.wait_ge(lo_done["u"], 1)
                dense(up_ps, "u", 0, 0)
                pe.wait_ge(t_lo_done, 2)
                pe.wait_ge(lo_done["g"], 1)
                lora(gate_ps, 0, 0, 0).then_inc(gate_done, 1)
                lora(up_ps, 1, 0, 0).then_inc(up_done, 1)

            def down(s, slot, start, stop):
                pe.wait_ge(lo_done["d"], s + 1)
                pe.wait_ge(h_lo_done, s + 1)
                w, h = (w_hi[slot], w_lo[slot]), (h_hi[slot], h_lo[slot])
                a = COLS["d"][0]
                for q in range(QUADS):
                    for part in h:
                        m = pe.matmul(td_ps[:, q * QT:(q + 1) * QT],
                                      ad_hl[slot][:, q, :, :].rearrange("p h r -> p (h r)"),
                                      part[:, q * QT:(q + 1) * QT], start=start and q == 0 and part is h[0],
                                      stop=stop, skip_group_check=True)
                if stop:
                    m.then_inc(td_done, 1)
                for j in range(TILES):
                    m = three(out_ps[j][:, :], cols(h, j * P, j * P + P), cols(w, a, a + D), start, False)
                m.then_inc(down_done, 1)

            def lora_down(g):
                pe.wait_ge(td_free, g + 2)
                pe.wait_ge(bd_lo_done, g + 1)
                for j in range(TILES):
                    for part in (bd_hi, bd_lo):
                        m = pe.matmul(out_ps[j][:, :], td_st[:, j * P:(j + 1) * P], part[:, j * P // QT, :],
                                      start=False, stop=part is bd_lo)
                    m.then_inc(out_done, 1)

            def mix_tile(g, j, bank=misc_ps):
                if j == 0:
                    pe.wait_ge(mix_in, (g + 1) * (16 * PER))
                pe.wait_ge(x1_done, g * TILES + (j + 1))
                if j and bank is misc_ps:
                    pe.wait_ge(y_done, g * TILES + j)
                pe.matmul(bank[:, :], mix[:, j, :], x1[:, j, :], start=True, stop=True).then_inc(mixed, 1)

            def lora_a(g, par):
                pe.wait_ge(xt_lo_done, g + 1)
                pe.wait_ge(aq_lo_done, g + 1)
                if not (isinstance(g, int) and g < 2):
                    pe.wait_ge(y_done, (g - 1) * TILES)
                for q in range(QUADS):
                    for k in range(KT):
                        a, b = (q * KT + k) * P, k * TOK + q * QT
                        st, mv = cols((aq_hi, aq_lo), a, a + P), cols((xt_hi[par], xt_lo[par]), b, b + QT)
                        for i, (x_, y_) in enumerate(((0, 0), (0, 1), (1, 0))):
                            m = pe.matmul(misc_ps[:, q * QT:(q + 1) * QT], st[x_], mv[y_],
                                          start=q == k == i == 0, stop=k == KT - 1 and i == 2,
                                          skip_group_check=True)
                m.then_inc(t_done, 1)

            def first():
                step_0()

            def chunk(g, par, c, cpar, fin, prep):
                s = g * CHUNKS + c
                at = c if isinstance(c, int) else -1
                if isinstance(s, int) and s == 0:
                    return
                gate(s, cpar, g, par, at)
                if fin and at in (1, 2):
                    mix_tile(g - 1, 0 if at == 1 else 3)
                if at == 0:
                    if fin:
                        down(s - 1, 1 - cpar, False, True)
                else:
                    if fin and at == 1:
                        pe.wait_ge(x1_done, g * TILES)
                        pe.wait_ge(td_masked, g)
                    down(s - 1, 1 - cpar, at == 1, False)
                if fin and at == 1:
                    mix_tile(g - 1, 1)
                up(s, cpar, par)
                if fin and at == 0:
                    lora_down(g - 1)
                if fin and at == 1:
                    mix_tile(g - 1, 2)
                if prep and at == 2:
                    lora_a(g + 1, 1 - par)

            def last():
                down(GROUPS * CHUNKS - 1, 1, False, True)
                lora_down(GROUPS - 1)
                for j in range(TILES):
                    mix_tile(GROUPS - 1, j, LAST_BANKS[j])

            run_groups(pe, chunk, first, last)


def kernel(x, itok_B_0_7, L0_cond_Wg, L0_cond_Wu, L0_cond_Wd, L0_cond_Ag, L0_cond_Bg, L0_cond_Au,
           L0_cond_Bu, L0_cond_Ad, L0_cond_Bd, L1_cond_weights):
    import numpy as np
    import concourse.bacc as bacc
    from concourse.bass_utils import run_bass_kernel_spmd

    ar = np.ascontiguousarray
    xf = np.asarray(x).reshape(GROUPS, TOK, D)

    def rows(w):
        return np.asarray(w).reshape(KT, P, CHUNKS, P).transpose(2, 1, 0, 3).reshape(CHUNKS, P, KT * P)

    def by_chunk(b):
        return np.asarray(b).reshape(ADAPTERS, RANK, CHUNKS, P)

    def lora_a(a, n):
        return np.asarray(a).reshape(ADAPTERS, n, P, RANK).transpose(2, 0, 1, 3)

    arrays = {
        "x": ar(xf.reshape(GROUPS, TILES, P, D).transpose(0, 2, 1, 3)),
        "xt": ar(xf.reshape(GROUPS, TOK, KT, P).transpose(0, 3, 2, 1).reshape(GROUPS, P, KT * TOK)),
        "idx": ar(np.asarray(itok_B_0_7).reshape(1, BATCH)),
        "packed": ar(np.concatenate([
            rows(L0_cond_Wg), rows(L0_cond_Wu), np.asarray(L0_cond_Wd).reshape(CHUNKS, P, D)], axis=2)),
        "a_gu": ar(np.stack([lora_a(L0_cond_Ag, KT), lora_a(L0_cond_Au, KT)], axis=3)
                   .reshape(P, ADAPTERS, KT * 2, RANK)),
        "a_d": ar(lora_a(L0_cond_Ad, CHUNKS)),
        "b_gu": ar(np.stack([by_chunk(L0_cond_Bg), by_chunk(L0_cond_Bu)], axis=3)
                   .reshape(ADAPTERS, RANK, CHUNKS * BW)),
        "b_d": ar(np.asarray(L0_cond_Bd)),
        "w1": ar(np.asarray(L1_cond_weights)),
        "slot_mask": (np.arange(P)[:, None] % QR // RANK == np.arange(PER)[None, :] % QS).astype(np.float32),
    }
    nc = bacc.Bacc("TRN2", target_bir_lowering=False, num_devices=1)
    args = [nc.dram_tensor(n, a.shape, mybir.dt.from_np(a.dtype), kind="ExternalInput").ap()
            for n, a in arrays.items()]
    out = nc.dram_tensor("y_out_dram", (GROUPS, P, TILES, D), F32, kind="ExternalOutput").ap()
    cond_resid_kernel(nc, *args, out)
    r = run_bass_kernel_spmd(nc, [arrays], core_ids=[0])
    y = r.results[0]["y_out_dram"]
    return y.transpose(0, 2, 1, 3).reshape(BATCH, SEQ, D)
```
